# Optimizing a Trainium2 kernel written in Bass

```python
import numpy as np
import jax
import jax.numpy as jnp

def _softmax(x, axis=-1):
    return jax.nn.softmax(x, axis=axis)
def _gelu(x):
    return jax.nn.gelu(x, approximate=True)
def _silu(x):
    return jax.nn.silu(x)
def _sigmoid(x):
    return jax.nn.sigmoid(x)
def _layernorm(x, axis=-1, eps=1e-5):
    m = jnp.mean(x, axis=axis, keepdims=True)
    v = jnp.var(x, axis=axis, keepdims=True)
    return (x - m) / jnp.sqrt(v + eps)
def _scatter_add(tgt, idx, src, axis=0):
    return tgt.at[idx].add(src)
def _segment_sum(src, seg, n):
    return jax.ops.segment_sum(src, seg, n)

kernel_name = 'mk_conv_seq_d2_conv_nchw512_101b3e'

def setup_inputs(seed: int = 0):
    np.random.seed(seed)
    _w = jnp.asarray
    def _rec_inputs():
        import jax
        import jax.numpy as jnp
        _gk = jax.random.key(seed)
        x = -0.0002928 + 1 * jax.random.normal(jax.random.fold_in(_gk, 1), (8, 512, 32, 32), jnp.float32)
        return x
    x = _rec_inputs()
    def _L0_conv_setup():
        import jax, jax.numpy as jnp
        import numpy as np
        NUM_HEADS = 8
        HEAD_DIM = 64
        GROUPS = 32
        EPS = 1e-05

        def _group_norm(x, w, b):
            B, C, H, W = x.shape
            xg = x.reshape(B, GROUPS, C // GROUPS, H, W)
            mu = xg.mean(axis=(2, 3, 4), keepdims=True)
            var = xg.var(axis=(2, 3, 4), keepdims=True)
            xn = ((xg - mu) * jax.lax.rsqrt(var + EPS)).reshape(B, C, H, W)
            return xn * w[None, :, None, None] + b[None, :, None, None]
        key = jax.random.key(seed)
        ks = jax.random.split(key, 7)
        B, C, H, W = (8, 512, 32, 32)
        x = jax.random.normal(ks[0], (B, C, H, W), dtype=jnp.float32)
        gn_w = jnp.ones((C,), dtype=jnp.float32)
        gn_b = jnp.zeros((C,), dtype=jnp.float32)
        qkv_w = jax.random.normal(ks[1], (3 * C, C), dtype=jnp.float32) * (1.0 / np.sqrt(C))
        qkv_b = jnp.zeros((3 * C,), dtype=jnp.float32)
        proj_w = jax.random.normal(ks[2], (C, C), dtype=jnp.float32) * (1.0 / np.sqrt(C))
        proj_b = jnp.zeros((C,), dtype=jnp.float32)
        return {'x': x, 'gn_w': gn_w, 'gn_b': gn_b, 'qkv_w': qkv_w, 'qkv_b': qkv_b, 'proj_w': proj_w, 'proj_b': proj_b}
    _L0_conv_all = _L0_conv_setup()
    _L0_conv_in = {k: v for k, v in _L0_conv_all.items() if k in ('gn_w', 'gn_b', 'qkv_w', 'qkv_b', 'proj_w', 'proj_b', )}
    del _L0_conv_all

    def _L1_conv_setup():
        import jax, jax.numpy as jnp
        import numpy as np
        K_TOP = 256
        LN_EPS = 1e-05

        def _layer_norm(x, w, b, eps=LN_EPS):
            m = x.mean(-1, keepdims=True)
            v = x.var(-1, keepdims=True)
            return (x - m) / jnp.sqrt(v + eps) * w + b
        key = jax.random.key(seed)
        ks = jax.random.split(key, 5)
        B, C, H, W = (16, 512, 48, 48)
        s = 1.0 / np.sqrt(C)
        x = jax.random.normal(ks[0], (B, C, H, W), jnp.float32)
        wq = jax.random.normal(ks[1], (C, C), jnp.float32) * s
        wk = jax.random.normal(ks[2], (C, C), jnp.float32) * s
        wv = jax.random.normal(ks[3], (C, C), jnp.float32) * s
        wo = jax.random.normal(ks[4], (C, C), jnp.float32) * s
        ln_w = jnp.ones((C,), jnp.float32)
        ln_b = jnp.zeros((C,), jnp.float32)
        return {'x': x, 'wq': wq, 'wk': wk, 'wv': wv, 'wo': wo, 'ln_w': ln_w, 'ln_b': ln_b}
    _L1_conv_all = _L1_conv_setup()
    _L1_conv_in = {k: v for k, v in _L1_conv_all.items() if k in ('wq', 'wk', 'wv', 'wo', 'ln_w', 'ln_b', )}
    del _L1_conv_all

    return {
        "x": x,
        "L0_conv_gn_w": _L0_conv_in["gn_w"],
        "L0_conv_gn_b": _L0_conv_in["gn_b"],
        "L0_conv_qkv_w": _L0_conv_in["qkv_w"],
        "L0_conv_qkv_b": _L0_conv_in["qkv_b"],
        "L0_conv_proj_w": _L0_conv_in["proj_w"],
        "L0_conv_proj_b": _L0_conv_in["proj_b"],
        "L1_conv_wq": _L1_conv_in["wq"],
        "L1_conv_wk": _L1_conv_in["wk"],
        "L1_conv_wv": _L1_conv_in["wv"],
        "L1_conv_wo": _L1_conv_in["wo"],
        "L1_conv_ln_w": _L1_conv_in["ln_w"],
        "L1_conv_ln_b": _L1_conv_in["ln_b"],
    }

def reference(x, L0_conv_gn_w, L0_conv_gn_b, L0_conv_qkv_w, L0_conv_qkv_b, L0_conv_proj_w, L0_conv_proj_b, L1_conv_wq, L1_conv_wk, L1_conv_wv, L1_conv_wo, L1_conv_ln_w, L1_conv_ln_b):
    import jax
    import jax.numpy as jnp
    def _L0_conv_ref(x, gn_w, gn_b, qkv_w, qkv_b, proj_w, proj_b):
        import jax, jax.numpy as jnp
        import numpy as np
        NUM_HEADS = 8
        HEAD_DIM = 64
        GROUPS = 32
        EPS = 1e-05

        def _group_norm(x, w, b):
            B, C, H, W = x.shape
            xg = x.reshape(B, GROUPS, C // GROUPS, H, W)
            mu = xg.mean(axis=(2, 3, 4), keepdims=True)
            var = xg.var(axis=(2, 3, 4), keepdims=True)
            xn = ((xg - mu) * jax.lax.rsqrt(var + EPS)).reshape(B, C, H, W)
            return xn * w[None, :, None, None] + b[None, :, None, None]
        B, C, H, W = x.shape
        N = H * W
        h = _group_norm(x, gn_w, gn_b)
        hf = h.reshape(B, C, N)
        qkv = jnp.einsum('oc,bcn->bon', qkv_w, hf) + qkv_b[None, :, None]
        qkv = qkv.reshape(B, 3, NUM_HEADS, HEAD_DIM, N)
        q, k, v = (qkv[:, 0], qkv[:, 1], qkv[:, 2])
        attn = jnp.einsum('bhdi,bhdj->bhij', q, k) * HEAD_DIM ** (-0.5)
        attn = jax.nn.softmax(attn, axis=-1)
        out = jnp.einsum('bhij,bhdj->bhdi', attn, v)
        out = out.reshape(B, C, N)
        out = jnp.einsum('oc,bcn->bon', proj_w, out) + proj_b[None, :, None]
        return x + out.reshape(B, C, H, W)

    def _L1_conv_ref(x, wq, wk, wv, wo, ln_w, ln_b):
        import jax, jax.numpy as jnp
        import numpy as np
        K_TOP = 256
        LN_EPS = 1e-05

        def _layer_norm(x, w, b, eps=LN_EPS):
            m = x.mean(-1, keepdims=True)
            v = x.var(-1, keepdims=True)
            return (x - m) / jnp.sqrt(v + eps) * w + b
        B, C, H, W = x.shape
        N = H * W
        k_actual = min(K_TOP, N)
        scale = C ** (-0.5)
        xf = x.reshape(B, C, N)
        q = jnp.einsum('oc,bcn->bon', wq, xf)
        kk = jnp.einsum('oc,bcn->bon', wk, xf)
        v = jnp.einsum('oc,bcn->bon', wv, xf)
        importance = jnp.nan_to_num(jnp.sum(xf * xf, axis=1), nan=0.0, posinf=0.0, neginf=0.0)
        _, topk_idx = jax.lax.top_k(importance, k_actual)
        idx = topk_idx[:, None, :]
        q_sel = jnp.take_along_axis(q, jnp.broadcast_to(idx, (B, C, k_actual)), axis=2).transpose(0, 2, 1)
        k_sel = jnp.take_along_axis(kk, jnp.broadcast_to(idx, (B, C, k_actual)), axis=2).transpose(0, 2, 1)
        v_sel = jnpp_take = jnp.take_along_axis(v, jnp.broadcast_to(idx, (B, C, k_actual)), axis=2).transpose(0, 2, 1)
        q_sel = _layer_norm(q_sel, ln_w, ln_b)
        k_sel = _layer_norm(k_sel, ln_w, ln_b)
        attn = jnp.einsum('bic,bjc->bij', q_sel, k_sel) * scale
        attn = jnp.nan_to_num(attn, nan=0.0, posinf=0.0, neginf=0.0)
        attn = jnp.clip(attn, -80.0, 80.0)
        attn = jax.nn.softmax(attn, axis=-1)
        attn = jnp.nan_to_num(attn, nan=0.0, posinf=0.0, neginf=0.0)
        attended = jnp.einsum('bij,bjc->bic', attn, v_sel)
        bi = jnp.arange(B)[:, None, None]
        ci = jnp.arange(C)[None, :, None]
        out = v.at[bi, ci, idx].set(attended.transpose(0, 2, 1))
        out = jnp.einsum('oc,bcn->bon', wo, out).reshape(B, C, H, W)
        return x + out

    def _gn(v, G=32, eps=1e-5):
        B_, C_, H_, W_ = v.shape
        g = v.reshape(B_, G, C_ // G, H_, W_)
        m = jnp.mean(g, axis=(2, 3, 4), keepdims=True)
        s = jnp.var(g, axis=(2, 3, 4), keepdims=True)
        return ((g - m) / jnp.sqrt(s + eps)).reshape(v.shape)

    def _ln_c(v, eps=1e-6):
        m = jnp.mean(v, axis=1, keepdims=True)
        s = jnp.var(v, axis=1, keepdims=True)
        return (v - m) / jnp.sqrt(s + eps)

    def _ln_t(v, eps=1e-5):
        m = jnp.mean(v, axis=-1, keepdims=True)
        s = jnp.var(v, axis=-1, keepdims=True)
        return (v - m) / jnp.sqrt(s + eps)

    def _to_tokens(v):
        B_, C_, H_, W_ = v.shape
        return v.reshape(B_, C_, H_ * W_).transpose(0, 2, 1)
    def _from_tokens(t, like):
        B_, C_, H_, W_ = like.shape
        return t.transpose(0, 2, 1).reshape(B_, C_, H_, W_)

    x = _L0_conv_ref(x, L0_conv_gn_w, L0_conv_gn_b, L0_conv_qkv_w, L0_conv_qkv_b, L0_conv_proj_w, L0_conv_proj_b)
    x = _L1_conv_ref(x, L1_conv_wq, L1_conv_wk, L1_conv_wv, L1_conv_wo, L1_conv_ln_w, L1_conv_ln_b)
    return x


_drawn_inputs = setup_inputs


def setup_inputs(seed=0):
    import zlib

    import numpy as np

    out = dict(_drawn_inputs(seed))
    spreads = {'L0_conv_gn_w': (1.0, 0.2),
     'L0_conv_gn_b': (0.0, 0.1),
     'L0_conv_qkv_b': (0.0, 0.1),
     'L0_conv_proj_b': (0.0, 0.1),
     'L1_conv_ln_w': (1.0, 0.6),
     'L1_conv_ln_b': (0.0, 0.8)}
    factors = {}
    for name, (base, spread) in spreads.items():
        noise = np.random.default_rng([zlib.crc32(name.encode()), seed]).standard_normal(out[name].shape)
        drawn = base * np.exp(spread * noise) if base else spread * noise
        out[name] = jnp.asarray(drawn.astype(out[name].dtype))
    for name, factor in factors.items():
        out[name] = (out[name] * factor).astype(out[name].dtype)
    return out
```

```python
from contextlib import ExitStack

import numpy as np

import concourse.bass as bass
from concourse import mybir

ALU = mybir.AluOpType
ACT = mybir.ActivationFunctionType
F32 = mybir.dt.float32
F32R = mybir.dt.float32r
AX_X = mybir.AxisListType.X

P = 128
HALF = 512
BATCH, C, N = 8, 512, 1024
CT = C // P
NT = N // P
HEADS, HD = 8, 64
PAIRS = HEADS // 2
GROUP = C // 32
GN_EPS = 1e-5
ATT_SCALE = HD ** -0.5


class Plan:

    def __init__(self, start, *phases):
        self.start, self.phases = start, phases
        self.names = [name for name, _ in phases]

    def ahead(self, phase):
        n = self.names.index(phase)
        return [self.names[n - 1]] * (n > 0) + [phase] * (self.phases[n][1] > 1)


LAYER0 = Plan(1, ("pro", 1), ("first", 1), ("mid", BATCH - 2), ("last", 1), ("epi", 1))
LAYER1 = Plan(0, ("pro", 1), ("mid", BATCH - 1), ("epi", 1))


class Tally:

    def __init__(self, plan, step=1, **phases):
        self.plan, self.step = plan, step
        self.phases = {name: phases.get(name, []) for name in plan.names}

    def before(self, phase, b):
        total = 0
        for name, times in self.plan.phases:
            one = len(self.phases[name]) * self.step
            if name == phase:
                return (b - self.plan.start) * one + total if times > 1 else total
            total += times * one

    def after(self, phase, b, key):
        return self.before(phase, b) + (self.phases[phase].index(key) + 1) * self.step

    def after_previous(self, phase, b, key):
        back = {len(self.phases[a]) - 1 - self.phases[a].index(key)
                for a in self.plan.ahead(phase) if key in self.phases[a]}
        assert len(back) == 1
        back = back.pop() * self.step
        assert self.before(phase, self.plan.start) > back
        return self.before(phase, b) - back

    def value(self, phase, b, key, previous):
        return self.after_previous(phase, b, key) if previous else self.after(phase, b, key)

    def back(self, phase, key, k=1, same=lambda w: True):
        own = self.phases[phase]
        found = [(False, w) for w in reversed(own[:own.index(key)]) if same(w)]
        for ahead in self.plan.ahead(phase):
            found += [(True, w) for w in reversed(self.phases[ahead]) if same(w)]
        return found[k - 1] if k <= len(found) else (None, None)


def blocks(p):
    return [(2 * p, 2 * p + 1), (2 * p + 1, 2 * p + 2 if p + 1 < PAIRS else None)]


def batch_order(out, nxt):
    units = [("o", t) for t in range(CT)] if out else []
    for p in range(PAIRS):
        units += [("at", 2 * p, j) for j in range(NT)]
        if p + 1 < PAIRS:
            units += [("v", p + 1), ("q", p + 1), ("k", p + 1), ("vt", p + 1)]
        units += [("at", 2 * p + 1, j) for j in range(NT)]
    if nxt:
        units += [("v", 0), ("q", 0), ("k", 0), ("vt", 0)]
    return units


UNITS = dict(pro=[("v", 0), ("q", 0), ("k", 0), ("vt", 0)], first=batch_order(False, True),
             mid=batch_order(True, True), last=batch_order(True, False), epi=[("o", t) for t in range(CT)])


def tally(want, step=1):
    return Tally(LAYER0, step, **{ph: [u for u in us if want(u)] for ph, us in UNITS.items()})


def per_head(keys=lambda h: [h]):
    one = [k for h in range(HEADS) for k in keys(h)]
    return Tally(LAYER0, first=one, mid=one, last=one)


def slot_of(h):
    return h % 3


PIECE_SLOT = {"v": lambda n: 0, "q": lambda n: 1, "k": lambda n: 2, "o": lambda t: (t + 3) % 4}
RAW_SLOT = {"v": lambda n: 0, "q": lambda n: 1, "k": lambda n: 0, "o": lambda t: (t + 1) % 2}


def attention_layer(nc, x, w_pieces, bias_half, bias_v, bias_o, gn_wb, x1, consts):
    ident, gmat, s_const = consts
    with ExitStack() as ctx:
        def sb(name, shape, dt=F32):
            return ctx.enter_context(nc.sbuf_tensor(name, shape, dt))

        def sem(name):
            return ctx.enter_context(nc.semaphore(name))

        raw = sb("w_raw", [P, 2, CT * P])
        wh = sb("w_high", [P, 4, CT * P], F32R)
        wl = sb("w_low", [P, 4, CT * P], F32R)
        xs = sb("x_tiles", [P, CT, N])
        hh = sb("h_high", [P, CT, N], F32R)
        hl = sb("h_low", [P, CT, N], F32R)
        k1 = sb("k_high_low", [P, 3, N], F32R)
        k2 = sb("k_high_one", [P, 3, N], F32R)
        q1 = sb("q_high_high", [P, 3, N], F32R)
        q2 = sb("q_low_max", [P, 3, N], F32R)
        v1 = sb("v_high", [P, 2, NT, 3, HD], F32R)
        v2 = sb("v_low", [P, 2, NT, 3, HD], F32R)
        ph = sb("p_high", [P, 2, N], F32R)
        pl = sb("p_low", [P, 2, N], F32R)
        p32 = sb("p_full", [P, N])
        num = sb("numerator", [P, N])
        den = sb("denominator", [P, N])
        oh = sb("o_high", [P, PAIRS, N], F32R)
        ol = sb("o_low", [P, PAIRS, N], F32R)
        v32 = sb("v_full", [P, N])
        mcol = sb("row_max", [P, 2, NT])
        bh = sb("bias_qk", [HD, 3 * HEADS])
        bv = sb("bias_v", [P, PAIRS])
        bo = sb("bias_o", [P, CT])
        gwb = sb("gn_weight_bias", [P, 2, CT])
        bst = sb("bn_parts", [P, 2, 6])
        mv = sb("mean_var", [P, CT, 2])
        carry = sb("carry", [P, 1])
        carry_p = sb("carry_pool", [P, 2])
        gs = sb("gn_small", [P, 8, CT])

        ring = ctx.enter_context(nc.psum_tensor("ring", [P, 2, N], F32))
        pmax = ctx.enter_context(nc.psum_tensor("pmax", [P, N], F32))
        pv = ctx.enter_context(nc.psum_tensor("pv", [P, N], F32))

        s_unit, s_max, s_rows, s_phu, s_plu, s_gmm = (
            sem(n) for n in ("s_unit", "s_max", "s_rows", "s_phu", "s_plu", "s_gmm"))
        s_ph, s_p32, s_qkh, s_twin, s_v32, s_vh, s_mrow, s_nd, s_oh, s_hh = (
            sem(n) for n in ("s_ph", "s_p32", "s_qkh", "s_twin", "s_v32", "s_vh", "s_mrow", "s_nd", "s_oh", "s_hh"))
        s_pl, s_mx, s_qkl, s_vl, s_x1, s_rec, s_on, s_bn, s_mv, s_gst, s_gab, s_h32, s_dset = (
            sem(n) for n in ("s_pl", "s_mx", "s_qkl", "s_vl", "s_x1", "s_rec", "s_on", "s_bn", "s_mv", "s_gst",
                             "s_gab", "s_h32", "s_dset"))
        s_wh, s_wl, s_ol, s_hl, s_rstd = (sem(n) for n in ("s_wh", "s_wl", "s_ol", "s_hl", "s_rstd"))
        s_raw = [sem(f"s_raw{i}") for i in range(2)]
        s_xin = [sem(f"s_xin{i}") for i in range(CT)]
        s_xout = [sem(f"s_xout{i}") for i in range(CT)]
        s_par, s_carry = sem("s_par"), sem("s_carry")

        unit = tally(lambda u: True)
        is_at = lambda u: u[0] == "at"
        at = tally(is_at)
        qk = tally(lambda u: u[0] in "qk")
        vv = tally(lambda u: u[0] == "v")
        vt = tally(lambda u: u[0] == "vt")
        oo = tally(lambda u: u[0] == "o")
        pieces = tally(lambda u: u[0] in ("v", "q", "k", "o"))
        heads = per_head()
        pairs = per_head(lambda h: [h // 2] if h % 2 else [])
        m_first = [(h, i) for h in range(HEADS) for i in range(NT)]
        maxes = Tally(LAYER0, first=m_first, mid=m_first, last=m_first)
        rows = per_head()

        def per_norm(one):
            return Tally(LAYER0, pro=one, first=one, mid=one)

        tiles = per_norm(list(range(CT)))
        bn2 = per_norm([(t, i) for t in range(CT) for i in range(2)])
        gmm = per_norm([0, 1])
        gst = per_norm(["dev", "sq", "esum", "var", "ws", "bs"])
        norm = per_norm([0])
        rec = per_head(lambda h: [h // 2] if h % 2 else [])
        xin = Tally(LAYER0, 16, pro=["x"], first=["x"], mid=["r", "x"], last=["r"], epi=["r"])
        xout = Tally(LAYER0, 16, mid=["s"], last=["s"], epi=["s"])
        raws = [tally(lambda u, i=i: u[0] in RAW_SLOT and RAW_SLOT[u[0]](u[1]) == i, 16) for i in range(2)]

        block = ctx.enter_context(nc.Block())

        @block.tensor
        def _(pe):
            mm = nc.tensor.matmul

            def free(ph_, b, u):
                n = UNITS[ph_].index(u)
                prev, w = unit.back(ph_, u, 2)
                if w is not None:
                    if w[0] == "at":
                        pe.wait_ge(s_p32, at.value(ph_, b, w, prev))
                    elif w[0] == "v":
                        pe.wait_ge(s_v32, vv.value(ph_, b, w, prev))
                    elif w[0] == "vt":
                        pe.wait_ge(s_vl, vt.value(ph_, b, w, prev))
                    elif w[0] == "o":
                        pe.wait_ge(s_x1, oo.value(ph_, b, w, prev))
                    else:
                        pe.wait_ge(s_qkl, qk.value(ph_, b, w, prev))
                return ring[:, n % 2, :]

            def project(ph_, b, u, high, low, last_channels=lambda: None):
                out = free(ph_, b, u)
                pe.wait_ge(s_wl, pieces.after(ph_, b, u))
                s = PIECE_SLOT[u[0]](u[1])
                for c in range(CT):
                    if c == CT - 1:
                        last_channels()
                    w1, w2 = wh[:, s, c * P:(c + 1) * P], wl[:, s, c * P:(c + 1) * P]
                    for i, (w, a) in enumerate(((w1, high), (w1, low), (w2, high))):
                        for n in range(2):
                            last = mm(out[:, n * HALF:(n + 1) * HALF], w, a[:, c, n * HALF:(n + 1) * HALF],
                                      start=(c == 0 and i == 0), stop=(c == CT - 1 and i == 2))
                last.then_inc(s_unit, 1)

            def turn_v(ph_, b, p):
                out = free(ph_, b, ("vt", p))
                pe.wait_ge(s_v32, vv.after(ph_, b, ("v", p)))
                for j in range(NT):
                    last = nc.tensor.transpose(out[:, j * P:(j + 1) * P], v32[:, j * P:(j + 1) * P], ident[:, :])
                last.then_inc(s_unit, 1)

            def first_pair_ready(ph_, b):
                pe.wait_ge(s_hl, tiles.after(ph_, b, CT - 1))
                pe.wait_ge(s_hh, tiles.after(ph_, b, CT - 1))

            def qk_ready(ph_, b, h):
                prev = h < 2
                pe.wait_ge(s_qkl, qk.value(ph_, b, ("k", h // 2), prev))
                pe.wait_ge(s_twin, qk.value(ph_, b, ("k", h // 2), prev))

            def take_max(ph_, b, h, i):
                if i == 0:
                    qk_ready(ph_, b, h)
                    if h > 0:
                        pe.wait_ge(s_mrow, rows.after(ph_, b, h - 1))
                    else:
                        pe.wait_ge(s_gst, gst.after_previous(ph_, b, "bs"))
                else:
                    pe.wait_ge(s_mx, maxes.after(ph_, b, (h, i - 1)))
                s = slot_of(h)
                for n in range(2):
                    last = mm(pmax[:, n * HALF:(n + 1) * HALF], q1[:, s, i * P:(i + 1) * P],
                              k1[:, s, n * HALF:(n + 1) * HALF], start=True, stop=True)
                last.then_inc(s_max, 1)

            def max_rows(ph_, b, h):
                pe.wait_ge(s_mx, maxes.after(ph_, b, (h, NT - 1)))
                for i in range(NT):
                    last = nc.tensor.transpose(pmax[0:1, i * P:(i + 1) * P], mcol[:, h % 2, i:i + 1], ident[:, :])
                last.then_inc(s_rows, 1)

            def scores(ph_, b, h, j):
                out = free(ph_, b, ("at", h, j))
                s = slot_of(h)
                keys = slice(j * P, (j + 1) * P)
                for n in range(2):
                    mm(out[:, n * HALF:(n + 1) * HALF], k1[:, s, keys], q1[:, s, n * HALF:(n + 1) * HALF],
                       start=True, stop=False)
                if j == 0:
                    pe.wait_ge(s_mrow, rows.after(ph_, b, h))
                for n in range(2):
                    last = mm(out[:, n * HALF:(n + 1) * HALF], k2[0:HD + 1, s, keys],
                              q2[0:HD + 1, s, n * HALF:(n + 1) * HALF], start=False, stop=True)
                last.then_inc(s_unit, 1)

            def weigh_high(ph_, b, h, j):
                if j == 0:
                    if h > 0:
                        pe.wait_ge(s_nd, heads.after(ph_, b, h - 1))
                    elif ph_ != "first":
                        pe.wait_ge(s_nd, heads.after_previous(ph_, b, HEADS - 1))
                    pe.wait_ge(s_vl, vt.value(ph_, b, ("vt", h // 2), h < 2))
                    pe.wait_ge(s_vh, vt.value(ph_, b, ("vt", h // 2), h < 2))
                a = h % 2
                pe.wait_ge(s_ph, at.after(ph_, b, ("at", h, j)))
                for i, v in enumerate((v1, v2)):
                    w = v[:, (h // 2) % 2, j, a:a + 2, :].rearrange("p a d -> p (a d)")
                    for n in range(2):
                        last = mm(pv[:, n * HALF:(n + 1) * HALF], w, ph[:, j % 2, n * HALF:(n + 1) * HALF],
                                  start=(j == 0 and i == 0), stop=False)
                last.then_inc(s_phu, 1)

            def weigh_low(ph_, b, h, j):
                a = h % 2
                w = v1[:, (h // 2) % 2, j, a:a + 2, :].rearrange("p a d -> p (a d)")
                pe.wait_ge(s_pl, at.after(ph_, b, ("at", h, j)))
                for n in range(2):
                    last = mm(pv[:, n * HALF:(n + 1) * HALF], w, pl[:, j % 2, n * HALF:(n + 1) * HALF],
                              start=False, stop=(j == NT - 1))
                last.then_inc(s_plu, 1)

            def finish_head(ph_, b, h):
                weigh_high(ph_, b, h, NT - 1)
                weigh_low(ph_, b, h, NT - 2)
                weigh_low(ph_, b, h, NT - 1)

            def group_sums(ph_, b, i):
                if i == 0:
                    pe.wait_ge(s_mv, tiles.after(ph_, b, CT - 1))
                    if ph_ != "pro":
                        pe.wait_ge(s_mrow, rows.after(ph_, b, HEADS - 1))
                    src = mv[:, :, 0]
                else:
                    pe.wait_ge(s_gst, gst.after(ph_, b, "esum"))
                    src = gs[:, 3, :]
                mm(pmax[:, i * 8:i * 8 + CT], gmat[:, :], src, start=True, stop=True).then_inc(s_gmm, 1)

            def attention_block(ph_, b, h, h_max, pending):
                for j in range(NT):
                    if h_max is not None:
                        take_max(ph_, b, h_max, j)
                    scores(ph_, b, h, j)
                    if j > 0:
                        weigh_high(ph_, b, h, j - 1)
                    elif pending is not None:
                        finish_head(ph_, b, pending)
                    if j > 1:
                        weigh_low(ph_, b, h, j - 2)
                    if h == HEADS - 1 and ph_ != "last" and j in (0, 1):
                        group_sums(ph_, b, j)
                if h_max is not None:
                    max_rows(ph_, b, h_max)

            def pair_projections(ph_, b, p, pending):
                project(ph_, b, ("v", p), hh, hl)
                if pending is not None:
                    finish_head(ph_, b, pending)
                project(ph_, b, ("q", p), hh, hl)
                project(ph_, b, ("k", p), hh, hl)
                turn_v(ph_, b, p)

            def output(ph_, b, t, with_max):
                def last_pair():
                    if with_max:
                        take_max(ph_, b, 0, 2 * t + 1)
                    if t == 0:
                        pe.wait_ge(s_oh, pairs.after_previous(ph_, b, PAIRS - 1))
                        pe.wait_ge(s_ol, pairs.after_previous(ph_, b, PAIRS - 1))

                if t == 0:
                    pe.wait_ge(s_ol, pairs.after_previous(ph_, b, PAIRS - 2))
                if with_max:
                    take_max(ph_, b, 0, 2 * t)
                project(ph_, b, ("o", t), oh, ol, last_pair)

            def batch(ph_, b, out, nxt):
                if out:
                    for t in range(CT):
                        output(ph_, b, t, True)
                else:
                    for i in range(NT):
                        take_max(ph_, b, 0, i)
                max_rows(ph_, b, 0)
                for p in range(PAIRS):
                    (ha, ma), (hb, mb) = blocks(p)
                    attention_block(ph_, b, ha, ma, ha - 1 if p else None)
                    if p + 1 < PAIRS:
                        pair_projections(ph_, b, p + 1, ha)
                        attention_block(ph_, b, hb, mb, None)
                    else:
                        attention_block(ph_, b, hb, mb, ha)
                if nxt:
                    first_pair_ready(ph_, b)
                    pair_projections(ph_, b, 0, HEADS - 1)
                else:
                    finish_head(ph_, b, HEADS - 1)

            pe.wait_ge(s_const, 5)
            group_sums("pro", 0, 0)
            group_sums("pro", 0, 1)
            pe.wait_ge(s_dset, 5)
            first_pair_ready("pro", 0)
            pair_projections("pro", 0, 0, None)
            batch("first", 0, False, True)
            with pe.Fori(1, BATCH - 1) as b:
                batch("mid", b, True, True)
            batch("last", BATCH - 1, True, False)
            for t in range(CT):
                output("epi", 0, t, False)

        @block.scalar
        def _(act):
            def exps(ph_, b, h, j):
                n = UNITS[ph_].index(("at", h, j))
                r = j % 2
                act.wait_ge(s_unit, unit.after(ph_, b, ("at", h, j)))
                prev, w = at.back(ph_, ("at", h, j), 2)
                if w is not None:
                    act.wait_ge(s_phu, at.value(ph_, b, w, prev))
                nc.scalar.activation(ph[:, r, :], ring[:, n % 2, :], ACT.Exp, scale=ATT_SCALE).then_inc(s_ph, 1)
                prev, w = at.back(ph_, ("at", h, j), 1)
                if w is not None:
                    act.wait_ge(s_pl, at.value(ph_, b, w, prev))
                nc.scalar.activation(p32[:, :], ring[:, n % 2, :], ACT.Exp, scale=ATT_SCALE).then_inc(s_p32, 1)

            def max_row(ph_, b, h):
                act.wait_ge(s_rows, rows.after(ph_, b, h))
                nc.scalar.mul(q2[HD:HD + 1, slot_of(h), :], pmax[0:1, :], -1.0).then_inc(s_mrow, 1)

            def qk_high(ph_, b, kind, p):
                n = UNITS[ph_].index((kind, p))
                act.wait_ge(s_unit, unit.after(ph_, b, (kind, p)))
                for a in range(2):
                    h = 2 * p + a
                    src = ring[a * HD:(a + 1) * HD, n % 2, :]
                    bias = bh[:, (HEADS if kind == "k" else 0) + h:(HEADS if kind == "k" else 0) + h + 1]
                    high = q1[0:HD] if kind == "q" else k1[0:HD]
                    last = nc.scalar.activation(high[:, slot_of(h), :], src, ACT.Identity, bias=bias)
                last.then_inc(s_qkh, 1)
                act.wait_ge(s_qkh, qk.after(ph_, b, (kind, p)))
                for a in range(2):
                    s = slot_of(2 * p + a)
                    high, twin = (q1[0:HD], q1[HD:P]) if kind == "q" else (k1[0:HD], k2[0:HD])
                    last = nc.scalar.activation(twin[:, s, :], high[:, s, :].bitcast(F32), ACT.Copy)
                last.then_inc(s_twin, 1)

            def v_full(ph_, b, p):
                n = UNITS[ph_].index(("v", p))
                act.wait_ge(s_unit, unit.after(ph_, b, ("v", p)))
                nc.scalar.activation(v32[:, :], ring[:, n % 2, :], ACT.Identity, bias=bv[:, p:p + 1]).then_inc(s_v32, 1)

            def v_high(ph_, b, p):
                n = UNITS[ph_].index(("vt", p))
                act.wait_ge(s_unit, unit.after(ph_, b, ("vt", p)))
                nc.scalar.activation(v1[:, p % 2, :, 0:3:2, :],
                                     ring[:, n % 2, :].rearrange("p (j a d) -> p j a d", j=NT, a=2),
                                     ACT.Copy).then_inc(s_vh, 1)

            def numer_denom(ph_, b, h):
                a = h % 2
                act.wait_ge(s_plu, at.after(ph_, b, ("at", h, NT - 1)))
                prev, w = pairs.back(ph_, h // 2)
                if a == 0 and w is not None:
                    act.wait_ge(s_ol, pairs.value(ph_, b, w, prev))
                mine, other = slice(a * HD, (a + 1) * HD), slice((1 - a) * HD, (2 - a) * HD)
                nc.scalar.activation(num[mine, :], pv[mine, :], ACT.Copy)
                nc.scalar.activation(den[mine, :], pv[other, :], ACT.Copy).then_inc(s_nd, 1)

            def o_high(ph_, b, p):
                act.wait_ge(s_on, pairs.after(ph_, b, p))
                nc.scalar.activation(oh[:, p, :], num[:, :], ACT.Copy).then_inc(s_oh, 1)

            def normed(ph_, b, t):
                if t == 0:
                    act.wait_ge(s_gab, norm.after(ph_, b, 0))
                    if ph_ != "pro":
                        act.wait_ge(s_unit, unit.after(ph_, b, ("k", PAIRS - 1)))
                a, c = gs[:, 6, t:t + 1], gs[:, 7, t:t + 1]
                nc.scalar.activation(hh[:, t, :], xs[:, t, :], ACT.Identity, bias=c, scale=a).then_inc(s_hh, 1)

            def attention_block(ph_, b, h, h_max, pending):
                for j in range(NT):
                    exps(ph_, b, h, j)
                    if j == 0 and pending is not None:
                        numer_denom(ph_, b, pending)
                    if h == HEADS - 1 and ph_ != "last" and 3 <= j <= 6:
                        normed(ph_, b, j - 3)
                if h_max is not None:
                    max_row(ph_, b, h_max)
                if h % 2 == 0 and h > 0:
                    o_high(ph_, b, h // 2 - 1)

            def pair_projections(ph_, b, p, pending):
                v_full(ph_, b, p)
                if pending is not None:
                    numer_denom(ph_, b, pending)
                qk_high(ph_, b, "q", p)
                qk_high(ph_, b, "k", p)
                v_high(ph_, b, p)

            def batch(ph_, b, out, nxt):
                max_row(ph_, b, 0)
                for p in range(PAIRS):
                    (ha, ma), (hb, mb) = blocks(p)
                    attention_block(ph_, b, ha, ma, ha - 1 if p else None)
                    if p + 1 < PAIRS:
                        pair_projections(ph_, b, p + 1, ha)
                        attention_block(ph_, b, hb, mb, None)
                    else:
                        attention_block(ph_, b, hb, mb, ha)
                if nxt:
                    pair_projections(ph_, b, 0, HEADS - 1)
                else:
                    numer_denom(ph_, b, HEADS - 1)
                o_high(ph_, b, PAIRS - 1)

            act.wait_ge(s_par, 16 * 4)
            for t in range(CT):
                normed("pro", 0, t)
            pair_projections("pro", 0, 0, None)
            batch("first", 0, False, True)
            with act.Fori(1, BATCH - 1) as b:
                batch("mid", b, True, True)
            batch("last", BATCH - 1, True, False)

        @block.vector
        def _(dve):
            stt, tt = nc.vector.scalar_tensor_tensor, nc.vector.tensor_tensor

            def reduce_max(ph_, b, h, i):
                dve.wait_ge(s_max, maxes.after(ph_, b, (h, i)))
                nc.vector.reduce_max(mcol[:, h % 2, i:i + 1], pmax[:, :], AX_X).then_inc(s_mx, 1)

            def p_low(ph_, b, h, j):
                r = j % 2
                dve.wait_ge(s_p32, at.after(ph_, b, ("at", h, j)))
                prev, w = at.back(ph_, ("at", h, j), 2)
                if w is not None:
                    dve.wait_ge(s_plu, at.value(ph_, b, w, prev))
                tt(pl[:, r, :], p32[:, :], ph[:, r, :].bitcast(F32), ALU.subtract).then_inc(s_pl, 1)

            def qk_low(ph_, b, kind, p):
                n = UNITS[ph_].index((kind, p))
                dve.wait_ge(s_qkh, qk.after(ph_, b, (kind, p)))
                for a in range(2):
                    h = 2 * p + a
                    col = (HEADS if kind == "k" else 0) + h
                    to = q2[0:HD] if kind == "q" else k1[HD:P]
                    high = q1[0:HD] if kind == "q" else k1[0:HD]
                    last = stt(out=to[:, slot_of(h), :], in0=ring[a * HD:(a + 1) * HD, n % 2, :],
                               scalar=bh[:, col:col + 1], in1=high[:, slot_of(h), :].bitcast(F32),
                               op0=ALU.add, op1=ALU.subtract)
                last.then_inc(s_qkl, 1)

            def v_low(ph_, b, p):
                n = UNITS[ph_].index(("vt", p))
                dve.wait_ge(s_vh, vt.after(ph_, b, ("vt", p)))
                tt(v2[:, p % 2, :, 0:3:2, :], ring[:, n % 2, :].rearrange("p (j a d) -> p j a d", j=NT, a=2),
                   v1[:, p % 2, :, 0:3:2, :].bitcast(F32), ALU.subtract).then_inc(s_vl, 1)

            def reciprocal(ph_, b, p, part, parts):
                if part == 0:
                    dve.wait_ge(s_nd, heads.after(ph_, b, 2 * p + 1))
                cols = slice(part * N // parts, (part + 1) * N // parts)
                r = nc.vector.reciprocal(den[:, cols], den[:, cols])
                if part == parts - 1:
                    r.then_inc(s_rec, 1)

            def normalise(ph_, b, p):
                dve.wait_ge(s_rec, rec.after(ph_, b, p))
                tt(num[:, :], num[:, :], den[:, :], ALU.mult).then_inc(s_on, 1)

            def tile_stats(ph_, b, t):
                dve.wait_ge(s_xin[t], xin.after(ph_, b, "x"))
                if ph_ != "pro" or t > 0:
                    if t > 0:
                        dve.wait_ge(s_mv, tiles.after(ph_, b, t - 1))
                for i in range(2):
                    nc.vector.bn_stats(bst[:, i, :], xs[:, t, i * HALF:(i + 1) * HALF]).then_inc(s_bn, 1)
                dve.wait_ge(s_bn, bn2.after(ph_, b, (t, 1)))
                nc.vector.memset(carry[:, :], 0.0)
                nc.vector.bn_aggr(mv[:, t, :], bst[:, :, :].rearrange("p a s -> p (a s)")).then_inc(s_mv, 1)

            def group_deviation(ph_, b):
                dve.wait_ge(s_gmm, gmm.after(ph_, b, 0))
                tt(gs[:, 1, :], pmax[:, 0:CT], mv[:, :, 0], ALU.subtract).then_inc(s_gst, 1)
                dve.wait_ge(s_gst, gst.after(ph_, b, "dev"))
                tt(gs[:, 2, :], gs[:, 1, :], gs[:, 1, :], ALU.mult).then_inc(s_gst, 1)
                dve.wait_ge(s_gst, gst.after(ph_, b, "sq"))
                tt(gs[:, 3, :], gs[:, 2, :], mv[:, :, 1], ALU.add).then_inc(s_gst, 1)

            def group_scale(ph_, b):
                dve.wait_ge(s_rstd, norm.after(ph_, b, 0))
                tt(gs[:, 6, :], gs[:, 5, :], gwb[:, 0, :], ALU.mult).then_inc(s_gst, 1)
                dve.wait_ge(s_gst, gst.after(ph_, b, "ws"))
                tt(gs[:, 2, :], pmax[:, 0:CT], gs[:, 6, :], ALU.mult).then_inc(s_gst, 1)
                dve.wait_ge(s_gst, gst.after(ph_, b, "bs"))
                tt(gs[:, 7, :], gwb[:, 1, :], gs[:, 2, :], ALU.subtract).then_inc(s_gab, 1)

            def normed_full(ph_, b, t):
                dve.wait_ge(s_hh, tiles.after(ph_, b, t))
                dve.wait_ge(s_gab, norm.after(ph_, b, 0))
                nc.vector.tensor_scalar(xs[:, t, :], xs[:, t, :], gs[:, 6, t:t + 1], gs[:, 7, t:t + 1],
                                        ALU.mult, ALU.add).then_inc(s_h32, 1)

            def attention_block(ph_, b, h, h_max, pending):
                for j in range(NT):
                    if h_max is not None:
                        reduce_max(ph_, b, h_max, j)
                    if j > 0:
                        p_low(ph_, b, h, j - 1)
                    elif pending is not None:
                        p_low(ph_, b, pending, NT - 1)
                    if h % 2 == 0 and h > 0 and 1 <= j <= 6:
                        reciprocal(ph_, b, h // 2 - 1, j - 1, 6)
                    if h % 2 == 0 and h > 0 and j == 7:
                        normalise(ph_, b, h // 2 - 1)
                    if h == HEADS - 2 and ph_ != "last" and j % 2 == 1:
                        tile_stats(ph_, b, j // 2)
                    if h == HEADS - 1 and ph_ != "last":
                        if j == 0:
                            group_deviation(ph_, b)
                        if j == 2:
                            variance_out(ph_, b)
                            group_scale(ph_, b)
                        if j >= 4:
                            normed_full(ph_, b, j - 4)

            def variance_out(ph_, b):
                dve.wait_ge(s_gmm, gmm.after(ph_, b, 1))
                nc.vector.tensor_scalar(gs[:, 4, :], pmax[:, 8:8 + CT], GN_EPS, None, ALU.add).then_inc(s_gst, 1)

            def pair_projections(ph_, b, p):
                qk_low(ph_, b, "q", p)
                qk_low(ph_, b, "k", p)
                v_low(ph_, b, p)

            def residual(ph_, b, t):
                n = UNITS[ph_].index(("o", t))
                dve.wait_ge(s_unit, unit.after(ph_, b, ("o", t)))
                dve.wait_ge(s_xin[t], xin.after(ph_, b, "r"))
                stt(out=xs[:, t, :], in0=ring[:, n % 2, :], scalar=bo[:, t:t + 1], in1=xs[:, t, :],
                    op0=ALU.add, op1=ALU.add).then_inc(s_x1, 1)

            def batch(ph_, b, out, nxt):
                if out:
                    for t in range(CT):
                        reduce_max(ph_, b, 0, 2 * t)
                        reduce_max(ph_, b, 0, 2 * t + 1)
                        residual(ph_, b, t)
                else:
                    for i in range(NT):
                        reduce_max(ph_, b, 0, i)
                for p in range(PAIRS):
                    (ha, ma), (hb, mb) = blocks(p)
                    attention_block(ph_, b, ha, ma, ha - 1 if p else None)
                    if p + 1 < PAIRS:
                        p_low(ph_, b, ha, NT - 1)
                        pair_projections(ph_, b, p + 1)
                        attention_block(ph_, b, hb, mb, None)
                    else:
                        attention_block(ph_, b, hb, mb, ha)
                p_low(ph_, b, HEADS - 1, NT - 1)
                for part in range(4):
                    reciprocal(ph_, b, PAIRS - 1, part, 4)
                normalise(ph_, b, PAIRS - 1)
                if nxt:
                    pair_projections(ph_, b, 0)

            nc.vector.memset(gs[:, 0, :], -0.5).then_inc(s_dset, 1)
            nc.vector.memset(k2[HD:HD + 1, :, :].bitcast(F32), 1.0).then_inc(s_dset, 1)
            nc.vector.memset(v1[:, :, :, 1, :].bitcast(F32), 1.0).then_inc(s_dset, 1)
            nc.vector.memset(v2[:, :, :, 1, :].bitcast(F32), 0.0).then_inc(s_dset, 1)
            nc.vector.memset(q2[HD:HD + 1, :, :].bitcast(F32), 0.0).then_inc(s_dset, 1)
            for t in range(CT):
                tile_stats("pro", 0, t)
            group_deviation("pro", 0)
            variance_out("pro", 0)
            dve.wait_ge(s_par, 16 * 4)
            group_scale("pro", 0)
            for t in range(CT):
                normed_full("pro", 0, t)
            pair_projections("pro", 0, 0)
            batch("first", 0, False, True)
            with dve.Fori(1, BATCH - 1) as b:
                batch("mid", b, True, True)
            batch("last", BATCH - 1, True, False)
            for t in range(CT):
                residual("epi", 0, t)

        @block.gpsimd
        def _(pool):
            def split_weights(ph_, b, u):
                r = RAW_SLOT[u[0]](u[1])
                s = PIECE_SLOT[u[0]](u[1])
                pool.wait_ge(s_raw[r], raws[r].after(ph_, b, u))
                prev, w = pieces.back(ph_, u, 1, lambda w: PIECE_SLOT[w[0]](w[1]) == s)
                if w is not None:
                    pool.wait_ge(s_unit, unit.value(ph_, b, w, prev))
                nc.gpsimd.tensor_tensor(carry_p[:, 0:1], carry_p[:, 1:2], carry_p[:, 1:2], ALU.add)
                nc.gpsimd.tensor_scalar(wh[:, s, :], raw[:, r, :], 1.0, 0.0, ALU.mult, ALU.add).then_inc(s_wh, 1)
                pool.wait_ge(s_wh, pieces.after(ph_, b, u))
                nc.gpsimd.tensor_tensor(wl[:, s, :], raw[:, r, :], wh[:, s, :].bitcast(F32),
                                        ALU.subtract).then_inc(s_wl, 1)

            def o_low(ph_, b, p, previous=False):
                pool.wait_ge(s_oh, pairs.value(ph_, b, p, previous))
                nc.gpsimd.tensor_tensor(ol[:, p, :], num[:, :], oh[:, p, :].bitcast(F32),
                                        ALU.subtract).then_inc(s_ol, 1)

            def rstd(ph_, b):
                pool.wait_ge(s_gst, gst.after(ph_, b, "var"))
                nc.gpsimd.tensor_tensor(gs[:, 5, :], gs[:, 4, :], gs[:, 0, :], ALU.pow).then_inc(s_rstd, 1)

            def h_low(ph_, b, t):
                pool.wait_ge(s_h32, tiles.after(ph_, b, t))
                nc.gpsimd.tensor_tensor(hl[:, t, :], xs[:, t, :], hh[:, t, :].bitcast(F32),
                                        ALU.subtract).then_inc(s_hl, 1)

            def output_pieces(ph_, b):
                for t in range(CT - 1):
                    split_weights(ph_, b, ("o", t))
                o_low(ph_, b, PAIRS - 1, True)
                split_weights(ph_, b, ("o", CT - 1))

            def batch(ph_, b, out, nxt):
                if out:
                    output_pieces(ph_, b)
                for p in range(1, PAIRS):
                    for kind in "vqk":
                        split_weights(ph_, b, (kind, p))
                    if p > 1:
                        o_low(ph_, b, p - 2)
                if nxt:
                    for kind in "vqk":
                        split_weights(ph_, b, (kind, 0))
                o_low(ph_, b, PAIRS - 2)
                if nxt:
                    rstd(ph_, b)
                    for t in range(CT):
                        h_low(ph_, b, t)

            nc.gpsimd.memset(carry_p[:, :], 0.0).then_inc(s_carry, 1)
            pool.wait_ge(s_carry, 1)
            for kind in "vqk":
                split_weights("pro", 0, (kind, 0))
            pool.wait_ge(s_dset, 1)
            rstd("pro", 0)
            for t in range(CT):
                h_low("pro", 0, t)
            batch("first", 0, False, True)
            with pool.Fori(1, BATCH - 1) as b:
                batch("mid", b, True, True)
            batch("last", BATCH - 1, True, False)
            output_pieces("epi", 0)

        @block.sync
        def _(sp):
            def load_piece(ph_, b, u):
                r = RAW_SLOT[u[0]](u[1])
                prev, w = raws[r].back(ph_, u)
                if w is not None:
                    sp.wait_ge(s_wl, pieces.value(ph_, b, w, prev))
                n = (["v", "q", "k", "o"].index(u[0])) * PAIRS + u[1]
                sp.dma_start(raw[:, r, :], w_pieces[n]).then_inc(s_raw[r], 16)

            def load_x(ph_, b, t, batch_index):
                if ph_ != "pro":
                    if ph_ == "first":
                        sp.wait_ge(s_hl, tiles.after_previous(ph_, b, t))
                    else:
                        sp.wait_ge(s_xout[t], xout.after(ph_, b, "s"))
                sp.dma_start(xs[:, t, :], x[batch_index, t * P:(t + 1) * P, :]).then_inc(s_xin[t], 16)

            def load_residual(ph_, b, t, batch_index):
                if ph_ in ("mid", "last"):
                    sp.wait_ge(s_hl, tiles.after_previous(ph_, b, t))
                else:
                    sp.wait_ge(s_xout[t], xout.after_previous(ph_, b, "s"))
                sp.dma_start(xs[:, t, :], x[batch_index, t * P:(t + 1) * P, :]).then_inc(s_xin[t], 16)

            def store(ph_, b, t, batch_index):
                sp.wait_ge(s_x1, oo.after(ph_, b, ("o", t)))
                sp.dma_start(x1[batch_index, t * P:(t + 1) * P, :], xs[:, t, :]).then_inc(s_xout[t], 16)

            def batch(ph_, b, out, nxt):
                if out:
                    load_piece(ph_, b, ("o", 0))
                    load_piece(ph_, b, ("o", 1))
                    for t in range(CT):
                        load_residual(ph_, b, t, b - 1)
                    load_piece(ph_, b, ("o", 2))
                    load_piece(ph_, b, ("o", 3))
                load_piece(ph_, b, ("v", 1))
                load_piece(ph_, b, ("q", 1))
                if out:
                    for t in range(CT):
                        store(ph_, b, t, b - 1)
                load_piece(ph_, b, ("k", 1))
                if nxt:
                    for t in range(CT):
                        load_x(ph_, b, t, b + 1)
                for p in list(range(2, PAIRS)) + ([0] if nxt else []):
                    for kind in "vqk":
                        load_piece(ph_, b, (kind, p))

            for t in range(CT):
                load_x("pro", 0, t, 0)
            load_piece("pro", 0, ("v", 0))
            load_piece("pro", 0, ("q", 0))
            sp.dma_start(bh[:, :], bias_half).then_inc(s_par, 16)
            sp.dma_start(bv[:, :], bias_v).then_inc(s_par, 16)
            sp.dma_start(bo[:, :], bias_o).then_inc(s_par, 16)
            sp.dma_start(gwb[:, :, :], gn_wb).then_inc(s_par, 16)
            load_piece("pro", 0, ("k", 0))
            batch("first", 0, False, True)
            with sp.Fori(1, BATCH - 1) as b:
                batch("mid", b, True, True)
            batch("last", BATCH - 1, True, False)
            load_piece("epi", 0, ("o", 0))
            load_piece("epi", 0, ("o", 1))
            for t in range(CT):
                load_residual("epi", 0, t, BATCH - 1)
            load_piece("epi", 0, ("o", 2))
            load_piece("epi", 0, ("o", 3))
            for t in range(CT):
                store("epi", 0, t, BATCH - 1)
            for t in range(CT):
                sp.wait_ge(s_xout[t], xout.after("epi", 0, "s"))

TOP = 256
RT = TOP // P
LN_EPS = 1e-5
TOP_SCALE = C ** -0.5
CLIP = 80.0
FINITE = 3.4028234663852886e38

CHOOSE = [("t", 0), ("t", 1), ("t", 2), ("t", 3), ("e", 1), ("rows", 0), ("e", 2), ("e", 3), ("st", 0), ("st", 1),
          ("x", 0), ("xs", 0), ("q", 0), ("k", 0), ("g", 0), ("qt", 0), ("kt", 0), ("s", 0), ("at", 0), ("u", 0)]
ORDER1 = dict(pro=[u for u in CHOOSE if u[0] != "e"], mid=[("e", 0)] + CHOOSE, epi=[("e", t) for t in range(CT)])
SLOTS1 = 4


def ring_slot(u):
    return ([("e", 0)] + CHOOSE).index(u) % SLOTS1


def tally1(want, step=1):
    return Tally(LAYER1, step, **{ph: [u for u in us if want(u)] for ph, us in ORDER1.items()})


ACT_LAST = {("st", 0), ("st", 1), ("x", 0), ("e", 1), ("e", 3)}


def combine_weights(nc, raw4, parts):
    wq, wk, ww, wd, ident = parts
    with ExitStack() as ctx:
        def sb(name, shape, dt=F32):
            return ctx.enter_context(nc.sbuf_tensor(name, shape, dt))

        def sem(name):
            return ctx.enter_context(nc.semaphore(name))

        raw = sb("raw_weights", [P, 4, CT, C])
        vp = sb("wv_parts", [P, 2, CT, C], F32R)
        op = sb("wo_parts", [P, 2, CT, C], F32R)
        diag = sb("diagonal", [P, CT, P])
        acc = ctx.enter_context(nc.psum_tensor("w_acc", [P, CT, C], F32))
        s_in = [sem(f"s_in{i}") for i in range(4)]
        s_high, s_low, s_prod, s_whigh, s_wlow, s_diag = (
            sem(n) for n in ("s_high", "s_low", "s_prod", "s_whigh", "s_wlow", "s_diag"))
        split = [vp, op, wq, wk]
        block = ctx.enter_context(nc.Block())

        @block.sync
        def _(sp):
            for i in range(4):
                sp.dma_start(raw[:, i, :, :], raw4[i]).then_inc(s_in[i], 16)

        @block.scalar
        def _(act):
            for i in range(4):
                act.wait_ge(s_in[i], 16)
                nc.scalar.activation(split[i][:, 0, :, :], raw[:, i, :, :], ACT.Copy).then_inc(s_high, 1)
            act.wait_ge(s_prod, 1)
            nc.scalar.activation(ww[:, 0, :, :], acc[:, :, :], ACT.Copy).then_inc(s_whigh, 1)
            act.wait_ge(s_diag, CT)
            nc.scalar.activation(wd[:, 0, :, :], diag[:, :, :], ACT.Copy).then_inc(s_whigh, 1)

        @block.vector
        def _(dve):
            for i in range(4):
                dve.wait_ge(s_high, i + 1)
                nc.vector.tensor_tensor(split[i][:, 1, :, :], raw[:, i, :, :], split[i][:, 0, :, :].bitcast(F32),
                                        ALU.subtract).then_inc(s_low, 1)
            dve.wait_ge(s_whigh, 1)
            for c in range(CT):
                nc.vector.tensor_tensor(diag[:, c, :], acc[:, c, c * P:(c + 1) * P], ident[:, :],
                                        ALU.add).then_inc(s_diag, 1)
            nc.vector.tensor_tensor(ww[:, 1, :, :], acc[:, :, :], ww[:, 0, :, :].bitcast(F32),
                                    ALU.subtract).then_inc(s_wlow, 1)
            dve.wait_ge(s_whigh, 2)
            nc.vector.tensor_tensor(wd[:, 1, :, :], diag[:, :, :], wd[:, 0, :, :].bitcast(F32),
                                    ALU.subtract).then_inc(s_wlow, 1)

        @block.tensor
        def _(pe):
            pe.wait_ge(s_low, 2)
            for c in range(CT):
                for m in range(CT):
                    for i, (a, b) in enumerate(((0, 0), (0, 1), (1, 0))):
                        last = nc.tensor.matmul(acc[:, c, :], vp[:, a, m, c * P:(c + 1) * P], op[:, b, m, :],
                                                start=(m == 0 and i == 0), stop=(m == CT - 1 and i == 2))
            last.then_inc(s_prod, 1)


def top_layer(nc, x1, y, raw4, ln_wb, shapes_only, ident):
    with ExitStack() as ctx:
        def sb(name, shape, dt=F32):
            return ctx.enter_context(nc.sbuf_tensor(name, shape, dt))

        def sem(name):
            return ctx.enter_context(nc.semaphore(name))

        wq = sb("wq_parts", [P, 2, CT, C], F32R)
        wk = sb("wk_parts", [P, 2, CT, C], F32R)
        ww = sb("w_parts", [P, 2, CT, C], F32R)
        wd = sb("w_diagonal_parts", [P, 2, CT, P], F32R)
        combine_weights(nc, raw4, (wq, wk, ww, wd, ident))

        x1f = sb("x1_full", [P, CT, N])
        xh = sb("x1_high", [P, CT, N], F32R)
        xl = sb("x1_low", [P, CT, N], F32R)
        work = sb("work", [P, 2, NT, C], F32R)
        late = work[:, :, :, :].rearrange("p a t c -> p (a t c)")

        def later(i, n):
            return late[:, i * C:i * C + n]

        q_t = [later(0, CT * TOP).rearrange("p (c r) -> p c r", c=CT), later(2, CT * TOP).rearrange("p (c r) -> p c r", c=CT)]
        k_t = [later(4, CT * TOP).rearrange("p (c r) -> p c r", c=CT), later(6, CT * TOP).rearrange("p (c r) -> p c r", c=CT)]
        g_p = [later(8, RT * C).rearrange("p (r c) -> p r c", r=RT), later(10, RT * C).rearrange("p (r c) -> p r c", r=RT)]
        a_t = [later(12, RT * TOP).rearrange("p (r c) -> p r c", r=RT), later(13, RT * TOP).rearrange("p (r c) -> p r c", r=RT)]
        sel = sb("chosen", [P, NT, TOP], F32R)
        selt = sb("chosen_t", [P, RT, N], F32R)
        xsel = sb("x_chosen", [P, RT, C])
        xsp = sb("x_chosen_parts", [P, 2, CT, TOP], F32R)
        qn = sb("q_normed", [P, RT, C])
        kn = sb("k_normed", [P, RT, C])
        up = sb("u_parts", [P, 2, RT, C], F32R)
        sc = sb("scores", [P, RT, TOP])
        ex = sb("exps", [P, RT, TOP])
        fin = sb("finite", [P, RT, TOP], mybir.dt.uint32)
        lnb = sb("ln_weight_bias", [P, 2, C])
        ranks = sb("rank_numbers", [P, TOP])
        lower = sb("lower_tokens", [P, P])
        junk = sb("junk", [P, 2, N + P], mybir.dt.bfloat16)
        junk_a = sb("junk_squares", [P, 2, C], mybir.dt.bfloat16)
        ys = sb("y_tiles", [P, 2, N])
        imp = sb("importance", [P, 2, NT])
        impf = sb("importance_finite", [P, NT], mybir.dt.uint32)
        cnt = sb("counts", [P, 5, NT])
        st = sb("ln_parts", [P, 2, 6])
        mv = sb("ln_mean_var", [P, RT, 2])
        rs = sb("ln_rstd", [P, 3, RT])
        carry = sb("carry1", [P, 1])
        sm = sb("softmax_small", [P, 4, RT])
        ring = ctx.enter_context(nc.psum_tensor("ring1", [P, SLOTS1, N], F32))

        s_unit, s_load_w = sem("s_unit1"), sem("s_load_w")
        a_th, a_sq, a_cp, a_hi, a_ex, a_xh = (sem(n) for n in ("a_th", "a_sq", "a_cp", "a_hi", "a_ex", "a_xh"))
        d_tl, d_imp, d_cnt, d_sel, d_lo, d_ln, d_sm, d_cp, d_set = (
            sem(n) for n in ("d_tl", "d_imp", "d_cnt", "d_sel", "d_lo", "d_ln", "d_sm", "d_cp", "d_set"))
        p_pow, p_xl = sem("p_pow"), sem("p_xl")
        s_in = [sem(f"s_x1in{t}") for t in range(CT)]
        s_out = [sem(f"s_yout{i}") for i in range(2)]

        unit = tally1(lambda u: True)
        tt_ = tally1(lambda u: u[0] == "t")
        cp = tally1(lambda u: u in ACT_LAST)
        dcp = tally1(lambda u: u in (("e", 0), ("e", 2)))
        LOWS = ("xs", "g", "qt", "kt", "at", "u")
        hl = tally1(lambda u: u[0] in LOWS)

        def choose_only(keys):
            return Tally(LAYER1, pro=keys, mid=keys)

        sq = choose_only(list(range(NT)))
        im = choose_only(["probe", "zero", "guard"])
        cn = choose_only([("c", t) for t in range(NT)] + ["s1", "s2"])
        se = choose_only([0])
        ln = choose_only([(w, k) for w in "qk" for k in ("s0", "a0", "s1", "a1", "eps", "w0", "b0", "w1", "b1")])
        pw = choose_only(["q", "k"])
        sf = choose_only(["scale", "probe", "zero", "guard", "clip", "max", "neg", "recip", "norm0", "norm1",
                          "less0", "less1"])
        ax = choose_only(list(range(RT)))
        xs_ = choose_only(list(range(CT)))
        xin = Tally(LAYER1, 16, pro=["x"], mid=["x"])
        yout = Tally(LAYER1, 16, pro=["free"], mid=[0, 1], epi=[0, 1])

        block = ctx.enter_context(nc.Block())

        @block.tensor
        def _(pe):
            mm, tr = nc.tensor.matmul, nc.tensor.transpose

            def free(ph_, b, u):
                prev, w = unit.back(ph_, u, 1, lambda w: ring_slot(w) == ring_slot(u))
                if w is not None:
                    if w in cp.phases["mid"]:
                        pe.wait_ge(a_cp, cp.value(ph_, b, w, prev))
                    elif w in dcp.phases["mid"]:
                        pe.wait_ge(d_cp, dcp.value(ph_, b, w, prev))
                    elif w[0] in LOWS:
                        pe.wait_ge(d_lo, hl.value(ph_, b, w, prev))
                    elif w[0] == "t":
                        pe.wait_ge(d_tl, tt_.value(ph_, b, w, prev))
                        pe.wait_ge(a_sq, sq.value(ph_, b, 2 * w[1] + 1, prev))
                    elif w[0] == "rows":
                        pe.wait_ge(d_cnt, cn.value(ph_, b, ("c", NT - 1), prev))
                    elif w[0] in "qk":
                        pe.wait_ge(d_ln, ln.value(ph_, b, (w[0], "w1"), prev))
                    else:
                        pe.wait_ge(d_sm, sf.value(ph_, b, "scale", prev))
                return ring[:, ring_slot(u), :]

            def parts(out, pairs, first=True, last=True):
                for n, (a, w) in enumerate(pairs):
                    done = mm(out, a, w, start=(first and n == 0), stop=(last and n == len(pairs) - 1))
                return done

            def to_tokens(ph_, b, i):
                out = free(ph_, b, ("t", i))
                if i == 0:
                    for c in range(CT):
                        pe.wait_ge(s_in[c], xin.after(ph_, b, "x"))
                for a in range(2):
                    for c in range(CT):
                        n = 2 * i + a
                        done = tr(out[:, a * C + c * P:a * C + (c + 1) * P], x1f[:, c, n * P:(n + 1) * P], ident[:, :])
                done.then_inc(s_unit, 1)

            def output(ph_, b, t):
                out = free(ph_, b, ("e", t))
                if t == 0:
                    pe.wait_ge(a_xh, xs_.after_previous(ph_, b, CT - 1))
                    pe.wait_ge(p_xl, xs_.after_previous(ph_, b, CT - 1))
                for c in range(CT):
                    for i, (a, w) in enumerate(((0, xh), (0, xl), (1, xh))):
                        l = wd[:, a, c, :] if c == t else ww[:, a, c, t * P:(t + 1) * P]
                        for n in range(2):
                            mm(out[:, n * HALF:(n + 1) * HALF], l, w[:, c, n * HALF:(n + 1) * HALF],
                               start=(c == 0 and i == 0), stop=False)
                if t == 0:
                    pe.wait_ge(d_lo, hl.after_previous(ph_, b, ("u", 0)))
                for r in range(RT):
                    for a in range(2):
                        for n in range(2):
                            done = mm(out[:, n * HALF:(n + 1) * HALF], up[:, a, r, t * P:(t + 1) * P],
                                      selt[:, r, n * HALF:(n + 1) * HALF], start=False,
                                      stop=(r == RT - 1 and a == 1))
                done.then_inc(s_unit, 1)

            def spread_importance(ph_, b):
                out = free(ph_, b, ("rows", 0))
                pe.wait_ge(d_imp, im.after(ph_, b, "guard"))
                for t in range(NT):
                    done = tr(out[:, t * P:(t + 1) * P], imp[:, 1, t:t + 1].broadcast_to([P, P]), ident[:, :])
                done.then_inc(s_unit, 1)

            def turn_chosen(ph_, b, r):
                out = free(ph_, b, ("st", r))
                pe.wait_ge(d_sel, se.after(ph_, b, 0))
                for t in range(NT):
                    done = tr(out[:, t * P:(t + 1) * P], sel[:, t, r * P:(r + 1) * P].bitcast(F32), ident[:, :])
                done.then_inc(s_unit, 1)

            def gather(ph_, b):
                out = free(ph_, b, ("x", 0))
                for r in range(RT):
                    for t in range(NT):
                        for a in range(2):
                            done = mm(out[:, r * C:(r + 1) * C], sel[:, t, r * P:(r + 1) * P], work[:, a, t, :],
                                      start=(t == 0 and a == 0), stop=(t == NT - 1 and a == 1))
                done.then_inc(s_unit, 1)

            def to_channels(ph_, b, u, src, ready):
                out = free(ph_, b, u)
                ready()
                for c in range(CT):
                    for r in range(RT):
                        done = tr(out[:, c * TOP + r * P:c * TOP + (r + 1) * P], src[:, r, c * P:(c + 1) * P],
                                  ident[:, :])
                done.then_inc(s_unit, 1)

            def project(ph_, b, u, w):
                out = free(ph_, b, u)
                if u[0] == "q":
                    pe.wait_ge(d_lo, hl.after(ph_, b, ("xs", 0)))
                for r in range(RT):
                    for c in range(CT):
                        l = [xsp[:, a, c, r * P:(r + 1) * P] for a in range(2)]
                        done = parts(out[:, r * C:(r + 1) * C],
                                     ((l[0], w[:, 0, c, :]), (l[0], w[:, 1, c, :]), (l[1], w[:, 0, c, :])),
                                     c == 0, c == CT - 1)
                done.then_inc(s_unit, 1)

            def top_scores(ph_, b):
                out = free(ph_, b, ("s", 0))
                pe.wait_ge(d_lo, hl.after(ph_, b, ("kt", 0)))
                for r in range(RT):
                    for c in range(CT):
                        l = [q_t[a][:, c, r * P:(r + 1) * P] for a in range(2)]
                        for n, (q_, k_) in enumerate(((0, 0), (0, 1), (1, 0))):
                            done = mm(out[:, r * HALF:r * HALF + TOP], l[q_], k_t[k_][:, c, :],
                                      start=(c == 0 and n == 0), stop=(c == CT - 1 and n == 2))
                done.then_inc(s_unit, 1)

            def turn_weights(ph_, b):
                out = free(ph_, b, ("at", 0))
                pe.wait_ge(d_sm, sf.after(ph_, b, "less1"))
                for j in range(RT):
                    for r in range(RT):
                        done = tr(out[:, j * TOP + r * P:j * TOP + (r + 1) * P], sc[:, r, j * P:(j + 1) * P],
                                  ident[:, :])
                done.then_inc(s_unit, 1)

            def change(ph_, b):
                out = free(ph_, b, ("u", 0))
                pe.wait_ge(d_lo, hl.after(ph_, b, ("at", 0)))
                for r in range(RT):
                    for j in range(RT):
                        l = [a_t[a][:, j, r * P:(r + 1) * P] for a in range(2)]
                        g = [g_p[a][:, j, :] for a in range(2)]
                        done = parts(out[:, r * C:(r + 1) * C], ((l[0], g[0]), (l[0], g[1]), (l[1], g[0])),
                                     j == 0, j == RT - 1)
                done.then_inc(s_unit, 1)

            def phase(ph_, b):
                for u in ORDER1[ph_]:
                    kind, n = u
                    if kind == "t":
                        to_tokens(ph_, b, n)
                    elif kind == "e":
                        output(ph_, b, n)
                    elif kind == "rows":
                        spread_importance(ph_, b)
                    elif kind == "st":
                        turn_chosen(ph_, b, n)
                    elif kind == "x":
                        gather(ph_, b)
                    elif kind == "xs":
                        to_channels(ph_, b, u, xsel, lambda: pe.wait_ge(a_cp, cp.after(ph_, b, ("x", 0))))
                    elif kind in "qkg":
                        project(ph_, b, u, dict(q=wq, k=wk, g=ww)[kind])
                    elif kind == "qt":
                        to_channels(ph_, b, u, qn, lambda: pe.wait_ge(d_ln, ln.after(ph_, b, ("q", "b1"))))
                    elif kind == "kt":
                        to_channels(ph_, b, u, kn, lambda: pe.wait_ge(d_ln, ln.after(ph_, b, ("k", "b1"))))
                    elif kind == "s":
                        top_scores(ph_, b)
                    elif kind == "at":
                        turn_weights(ph_, b)
                    else:
                        change(ph_, b)

            phase("pro", 0)
            with pe.Fori(0, BATCH - 1) as b:
                phase("mid", b)
            phase("epi", 0)

        @block.scalar
        def _(act):
            act_ = nc.scalar.activation

            def flat(ap):
                return ap.rearrange("p a b -> p (a b)")

            high_of = dict(xs=flat(xsp[:, 0, :, :]), g=flat(g_p[0]), qt=flat(q_t[0]), kt=flat(k_t[0]),
                           at=flat(a_t[0]), u=flat(up[:, 0, :, :]))

            def tokens(ph_, b, i):
                src = ring[:, ring_slot(("t", i)), :]
                act.wait_ge(s_unit, unit.after(ph_, b, ("t", i)))
                act_(work[:, 0, 2 * i:2 * i + 2, :].rearrange("p t c -> p (t c)"), src, ACT.Copy).then_inc(a_th, 1)
                for a in range(2):
                    prev, w = sq.back(ph_, 2 * i + a, 2)
                    if w is not None:
                        act.wait_ge(a_sq, sq.value(ph_, b, w, prev))
                    act_(junk_a[:, a, :], src[:, a * C:(a + 1) * C], ACT.Square,
                         accum_out=imp[:, 0, 2 * i + a:2 * i + a + 1]).then_inc(a_sq, 1)

            def copy(ph_, b, u):
                src = ring[:, ring_slot(u), :]
                act.wait_ge(s_unit, unit.after(ph_, b, u))
                if u[0] == "st":
                    act_(selt[:, u[1], :], src, ACT.Copy).then_inc(a_cp, 1)
                elif u[0] == "x":
                    act_(flat(xsel[:, :, :]), src, ACT.Copy).then_inc(a_cp, 1)
                else:
                    prev, w = cp.back(ph_, u, 1, lambda w: w[0] == "e")
                    if w is not None:
                        act.wait_ge(s_out[1], yout.value(ph_, b, 0 if w[1] == 1 else 1, prev))
                    act_(ys[:, 1, :], src, ACT.Copy).then_inc(a_cp, 1)

            def high(ph_, b, u):
                src = ring[:, ring_slot(u), :]
                to = high_of[u[0]]
                act.wait_ge(s_unit, unit.after(ph_, b, u))
                act_(to, src[:, 0:to.shape[1]], ACT.Copy).then_inc(a_hi, 1)

            def exps(ph_, b):
                act.wait_ge(d_sm, sf.after(ph_, b, "neg"))
                for r in range(RT):
                    act_(ex[:, r, :], sc[:, r, :], ACT.Exp, bias=sm[:, 0, r:r + 1],
                         accum_out=sm[:, 1, r:r + 1]).then_inc(a_ex, 1)

            def x_high(ph_, b, c):
                act_(xh[:, c, :], x1f[:, c, :], ACT.Copy).then_inc(a_xh, 1)

            def phase(ph_, b):
                for u in ORDER1[ph_]:
                    if u[0] == "t":
                        tokens(ph_, b, u[1])
                    elif u in ACT_LAST:
                        copy(ph_, b, u)
                        if u == ("x", 0):
                            for c in range(CT):
                                x_high(ph_, b, c)
                    elif u[0] in LOWS:
                        if u[0] == "at":
                            exps(ph_, b)
                        high(ph_, b, u)

            phase("pro", 0)
            with act.Fori(0, BATCH - 1) as b:
                phase("mid", b)
            phase("epi", 0)

        @block.vector
        def _(dve):
            v = nc.vector

            def flat(ap):
                return ap.rearrange("p a b -> p (a b)")

            parts_of = dict(xs=[flat(xsp[:, i, :, :]) for i in range(2)], g=[flat(g) for g in g_p],
                            qt=[flat(g) for g in q_t], kt=[flat(g) for g in k_t], at=[flat(g) for g in a_t],
                            u=[flat(up[:, i, :, :]) for i in range(2)])

            def tokens_low(ph_, b, i):
                dve.wait_ge(a_th, tt_.after(ph_, b, ("t", i)))
                dve.wait_ge(a_sq, sq.after(ph_, b, 2 * i + 1))
                v.tensor_tensor(work[:, 1, 2 * i:2 * i + 2, :].rearrange("p t c -> p (t c)"),
                                ring[:, ring_slot(("t", i)), :],
                                work[:, 0, 2 * i:2 * i + 2, :].rearrange("p t c -> p (t c)").bitcast(F32),
                                ALU.subtract).then_inc(d_tl, 1)

            def guard(ph_, b):
                v.tensor_scalar(impf[:, :], imp[:, 0, :], 0.0, 0.0, ALU.mult, ALU.is_equal).then_inc(d_imp, 1)
                v.memset(imp[:, 1, :], 0.0).then_inc(d_imp, 1)
                dve.wait_ge(d_imp, im.after(ph_, b, "zero"))
                v.memset(carry[:, :], 0.0)
                v.copy_predicated(imp[:, 1, :], impf[:, :], imp[:, 0, :]).then_inc(d_imp, 1)

            def count(ph_, b, t):
                src = ring[:, ring_slot(("rows", 0)), :]
                if t == 0:
                    dve.wait_ge(s_unit, unit.after(ph_, b, ("rows", 0)))
                mine = imp[:, 1, t:t + 1]
                ones = junk[:, t % 2, :]
                if t > 1:
                    dve.wait_ge(d_cnt, cn.after(ph_, b, ("c", t - 2)))
                if t > 0:
                    v.tensor_scalar(ones[:, 0:t * P], src[:, 0:t * P], mine, 0.0, ALU.is_ge, ALU.add,
                                    accum_out=cnt[:, 0, t:t + 1])
                v.tensor_scalar(ones[:, t * P:N], src[:, t * P:N], mine, 0.0, ALU.is_gt, ALU.add,
                                accum_out=cnt[:, 1, t:t + 1])
                v.scalar_tensor_tensor(out=ones[:, N:N + P], in0=src[:, t * P:(t + 1) * P], scalar=mine,
                                       in1=lower[:, :], op0=ALU.is_equal, op1=ALU.mult,
                                       accum_out=cnt[:, 2, t:t + 1]).then_inc(d_cnt, 1)

            def choose(ph_, b):
                dve.wait_ge(d_cnt, cn.after(ph_, b, ("c", NT - 1)))
                v.tensor_tensor(cnt[:, 3, :], cnt[:, 0, :], cnt[:, 1, :], ALU.add).then_inc(d_cnt, 1)
                dve.wait_ge(d_cnt, cn.after(ph_, b, "s1"))
                v.tensor_tensor(cnt[:, 4, :], cnt[:, 2, :], cnt[:, 3, :], ALU.add).then_inc(d_cnt, 1)
                dve.wait_ge(d_cnt, cn.after(ph_, b, "s2"))
                for t in range(NT):
                    done = v.tensor_scalar(sel[:, t, :], ranks[:, :], cnt[:, 4, t:t + 1], None, ALU.is_equal)
                done.then_inc(d_sel, 1)

            def low(ph_, b, u):
                to = parts_of[u[0]]
                dve.wait_ge(a_hi, hl.after(ph_, b, u))
                v.tensor_tensor(to[1], ring[:, ring_slot(u), 0:to[0].shape[1]], to[0].bitcast(F32),
                                ALU.subtract).then_inc(d_lo, 1)

            def layer_norm(ph_, b, w):
                src, to = ring[:, ring_slot((w, 0)), :], qn if w == "q" else kn
                dve.wait_ge(s_unit, unit.after(ph_, b, (w, 0)))
                for r in range(RT):
                    v.bn_stats(st[:, r, :], src[:, r * C:(r + 1) * C]).then_inc(d_ln, 1)
                    dve.wait_ge(d_ln, ln.after(ph_, b, (w, f"s{r}")))
                    v.memset(carry[:, :], 0.0)
                    v.bn_aggr(mv[:, r, :], st[:, r, :]).then_inc(d_ln, 1)
                dve.wait_ge(d_ln, ln.after(ph_, b, (w, "a1")))
                v.tensor_scalar(rs[:, 0, :], mv[:, :, 1], LN_EPS, None, ALU.add).then_inc(d_ln, 1)
                dve.wait_ge(p_pow, pw.after(ph_, b, w))
                for r in range(RT):
                    v.scalar_tensor_tensor(out=to[:, r, :], in0=src[:, r * C:(r + 1) * C], scalar=mv[:, r, 0:1],
                                           in1=lnb[:, 0, :], op0=ALU.subtract, op1=ALU.mult).then_inc(d_ln, 1)
                    dve.wait_ge(d_ln, ln.after(ph_, b, (w, f"w{r}")))
                    v.scalar_tensor_tensor(out=to[:, r, :], in0=to[:, r, :], scalar=rs[:, 1, r:r + 1],
                                           in1=lnb[:, 1, :], op0=ALU.mult, op1=ALU.add).then_inc(d_ln, 1)

            def softmax_in(ph_, b):
                src = ring[:, ring_slot(("s", 0)), :].rearrange("p (r c) -> p r c", r=RT)[:, :, 0:TOP]
                step = lambda k: dve.wait_ge(d_sm, sf.after(ph_, b, k))
                dve.wait_ge(s_unit, unit.after(ph_, b, ("s", 0)))
                v.tensor_scalar(ex[:, :, :], src, TOP_SCALE, None, ALU.mult).then_inc(d_sm, 1)
                step("scale")
                v.tensor_scalar(fin[:, :, :], ex[:, :, :], 0.0, 0.0, ALU.mult, ALU.is_equal).then_inc(d_sm, 1)
                v.memset(sc[:, :, :], 0.0).then_inc(d_sm, 1)
                step("zero")
                v.memset(carry[:, :], 0.0)
                v.copy_predicated(sc[:, :, :], fin[:, :, :], ex[:, :, :]).then_inc(d_sm, 1)
                step("guard")
                v.tensor_scalar(sc[:, :, :], sc[:, :, :], CLIP, -CLIP, ALU.min, ALU.max).then_inc(d_sm, 1)
                step("clip")
                v.reduce_max(sm[:, 3, :], sc[:, :, :], AX_X).then_inc(d_sm, 1)
                step("max")
                v.tensor_scalar(sm[:, 0, :], sm[:, 3, :], -1.0, None, ALU.mult).then_inc(d_sm, 1)

            def softmax_out(ph_, b):
                step = lambda k: dve.wait_ge(d_sm, sf.after(ph_, b, k))
                dve.wait_ge(a_ex, ax.after(ph_, b, RT - 1))
                v.reciprocal(sm[:, 2, :], sm[:, 1, :]).then_inc(d_sm, 1)
                step("recip")
                for r in range(RT):
                    v.tensor_scalar(sc[:, r, :], ex[:, r, :], sm[:, 2, r:r + 1], None, ALU.mult).then_inc(d_sm, 1)
                step("norm1")
                for r in range(RT):
                    v.tensor_tensor(sc[:, r, r * P:(r + 1) * P], sc[:, r, r * P:(r + 1) * P], ident[:, :],
                                    ALU.subtract).then_inc(d_sm, 1)

            def copy(ph_, b, u):
                dve.wait_ge(s_unit, unit.after(ph_, b, u))
                prev, w = dcp.back(ph_, u)
                if w is not None:
                    dve.wait_ge(s_out[0], yout.value(ph_, b, w[1] // 2, prev))
                v.tensor_copy(ys[:, 0, :], ring[:, ring_slot(u), :]).then_inc(d_cp, 1)

            def phase(ph_, b):
                for u in ORDER1[ph_]:
                    if u[0] == "t":
                        tokens_low(ph_, b, u[1])
                        if u[1] == 3:
                            guard(ph_, b)
                    elif u in dcp.phases["mid"]:
                        copy(ph_, b, u)
                    elif u[0] == "rows":
                        for t in range(NT // 2):
                            count(ph_, b, t)
                    elif u == ("st", 0):
                        for t in range(NT // 2, NT):
                            count(ph_, b, t)
                        choose(ph_, b)
                    elif u[0] in "qk" and len(u[0]) == 1:
                        layer_norm(ph_, b, u[0])
                    elif u[0] == "s":
                        softmax_in(ph_, b)
                    elif u[0] in LOWS:
                        if u[0] == "at":
                            softmax_out(ph_, b)
                        low(ph_, b, u)

            v.memset(cnt[:, 0, 0:1], 0.0).then_inc(d_set, 1)
            v.memset(rs[:, 2, :], -0.5).then_inc(d_set, 1)
            dve.wait_ge(s_load_w, 16 * 4)
            phase("pro", 0)
            with dve.Fori(0, BATCH - 1) as b:
                phase("mid", b)
            phase("epi", 0)

        @block.gpsimd
        def _(pool):
            def phase(ph_, b):
                for c in range(CT):
                    pool.wait_ge(a_xh, xs_.after(ph_, b, c))
                    nc.gpsimd.tensor_tensor(xl[:, c, :], x1f[:, c, :], xh[:, c, :].bitcast(F32),
                                            ALU.subtract).then_inc(p_xl, 1)
                    if c in (1, 2):
                        w = "qk"[c - 1]
                        pool.wait_ge(d_ln, ln.after(ph_, b, (w, "eps")))
                        nc.gpsimd.tensor_tensor(rs[:, 1, :], rs[:, 0, :], rs[:, 2, :], ALU.pow).then_inc(p_pow, 1)

            pool.wait_ge(d_set, 2)
            phase("pro", 0)
            with pool.Fori(0, BATCH - 1) as b:
                phase("mid", b)

        @block.sync
        def _(sp):
            def load(ph_, b, index):
                for c in range(CT):
                    if ph_ != "pro":
                        sp.wait_ge(p_xl, xs_.after_previous(ph_, b, c))
                    sp.dma_start(x1f[:, c, :], x1[index, c * P:(c + 1) * P, :]).then_inc(s_in[c], 16)

            def store(ph_, b, index):
                for t in range(CT):
                    if t % 2:
                        sp.wait_ge(a_cp, cp.after(ph_, b, ("e", t)))
                    else:
                        sp.wait_ge(d_cp, dcp.after(ph_, b, ("e", t)))
                    sp.dma_start(y[index, t * P:(t + 1) * P, :], ys[:, t % 2, :]).then_inc(s_out[t % 2], 16)

            sp.dma_start(lnb[:, 0, :], ln_wb[0:1, :].broadcast_to([P, C])).then_inc(s_load_w, 16)
            sp.dma_start(lnb[:, 1, :], ln_wb[1:2, :].broadcast_to([P, C])).then_inc(s_load_w, 16)
            sp.dma_start(ranks[:, :], shapes_only[:, 0:TOP]).then_inc(s_load_w, 16)
            sp.dma_start(lower[:, :], shapes_only[:, TOP:TOP + P]).then_inc(s_load_w, 16)
            for i in range(2):
                sp.sem_inc(s_out[i], 16)
            load("pro", 0, 0)
            with sp.Fori(0, BATCH - 1) as b:
                load("mid", b, b + 1)
                store("mid", b, b)
            store("epi", 0, BATCH - 1)
            for i in range(2):
                sp.wait_ge(s_out[i], yout.after("epi", 0, 1))


def make_constants(nc, ctx):
    ident = ctx.enter_context(nc.sbuf_tensor("identity", [P, P], F32))
    gmat = ctx.enter_context(nc.sbuf_tensor("group_mean", [P, P], F32))
    s_const = ctx.enter_context(nc.semaphore("s_const"))
    with nc.Block() as block:
        @block.gpsimd
        def _(pool):
            nc.gpsimd.memset(ident[:, :], 0.0).then_inc(s_const, 1)
            nc.gpsimd.memset(gmat[:, :], 1.0 / GROUP).then_inc(s_const, 1)
            pool.wait_ge(s_const, 2)
            nc.gpsimd.affine_select(out=ident[:, :], in_=ident[:, :], compare_op=ALU.not_equal, fill=1.0, base=0,
                                    pattern=[[-1, P]], channel_multiplier=1).then_inc(s_const, 1)
            g = gmat[:, :].rearrange("p (g c) -> p g c", c=GROUP)
            nc.gpsimd.affine_select(out=g, in_=g, compare_op=ALU.is_ge, fill=0.0, base=0,
                                    pattern=[[-GROUP, P // GROUP], [0, GROUP]],
                                    channel_multiplier=1).then_inc(s_const, 1)
            pool.wait_ge(s_const, 4)
            nc.gpsimd.affine_select(out=g, in_=g, compare_op=ALU.is_ge, fill=0.0, base=GROUP - 1,
                                    pattern=[[GROUP, P // GROUP], [0, GROUP]],
                                    channel_multiplier=-1).then_inc(s_const, 1)
    return ident, gmat, s_const


def _pieces(w):
    o = w.shape[0] // P
    return np.ascontiguousarray(w.reshape(o, P, CT, P).transpose(0, 3, 2, 1).reshape(o, P, CT * P))


def _rows(w):
    return np.ascontiguousarray(w.reshape(CT, P, w.shape[1]).transpose(1, 0, 2))


def kernel(**inputs):
    import concourse.bacc as bacc
    from concourse.bass_utils import run_bass_kernel_spmd

    a = {name: np.asarray(v) for name, v in inputs.items()}
    qkv_b = a["L0_conv_qkv_b"]
    columns = lambda v: np.ascontiguousarray(v.reshape(CT, P).T)
    order = np.arange(P)
    arrays = dict(
        x=np.ascontiguousarray(a["x"].reshape(BATCH, C, N)),
        pieces=np.concatenate([_pieces(a["L0_conv_qkv_w"][2 * C:]), _pieces(a["L0_conv_qkv_w"][:2 * C]),
                               _pieces(a["L0_conv_proj_w"])]),
        bias_half=np.ascontiguousarray(qkv_b.reshape(3 * HEADS, HD).T),
        bias_v=columns(qkv_b[2 * C:]),
        bias_o=columns(a["L0_conv_proj_b"]),
        gn_wb=np.ascontiguousarray(np.stack([columns(a["L0_conv_gn_w"]), columns(a["L0_conv_gn_b"])], 1)),
        raw4=np.stack([_rows(a["L1_conv_wv"]), _rows(a["L1_conv_wo"].T), _rows(a["L1_conv_wq"].T),
                       _rows(a["L1_conv_wk"].T)]),
        ln_wb=np.stack([a["L1_conv_ln_w"], a["L1_conv_ln_b"]]),
        shapes=np.concatenate([np.tile(np.arange(TOP), (P, 1)), order[None, :] < order[:, None]],
                              1).astype(np.float32),
    )
    nc = bacc.Bacc("TRN2", target_bir_lowering=False, num_devices=1)
    ap = {name: nc.dram_tensor(f"in_{name}", v.shape, F32, kind="ExternalInput").ap() for name, v in arrays.items()}
    out = nc.dram_tensor("out", [BATCH, C, N], F32, kind="ExternalOutput").ap()
    x1 = nc.dram_tensor("x1", [BATCH, C, N], F32).ap()
    with ExitStack() as ctx:
        ident, gmat, s_const = make_constants(nc, ctx)
        attention_layer(nc, ap["x"], ap["pieces"], ap["bias_half"], ap["bias_v"], ap["bias_o"], ap["gn_wb"], x1,
                        (ident, gmat, s_const))
        top_layer(nc, x1, out, ap["raw4"], ap["ln_wb"], ap["shapes"], ident)
    r = run_bass_kernel_spmd(nc, [{f"in_{name}": v for name, v in arrays.items()}], core_ids=[0])
    return r.results[0]["out"].reshape(a["x"].shape)
```
